# Optimizing a Trainium2 kernel written in Bass

```python
import numpy as np
import jax
import jax.numpy as jnp

def _softmax(x, axis=-1):
    return jax.nn.softmax(x, axis=axis)

def _gelu(x):
    return jax.nn.gelu(x, approximate=True)

def _silu(x):
    return jax.nn.silu(x)

def _sigmoid(x):
    return jax.nn.sigmoid(x)

def _layernorm(x, axis=-1, eps=1e-05):
    m = jnp.mean(x, axis=axis, keepdims=True)
    v = jnp.var(x, axis=axis, keepdims=True)
    return (x - m) / jnp.sqrt(v + eps)

def _scatter_add(tgt, idx, src, axis=0):
    return tgt.at[idx].add(src)

def _segment_sum(src, seg, n):
    return jax.ops.segment_sum(src, seg, n)
kernel_name = 'mk_conv_seq_d2_conv_nchw512_r4_034d18'

def setup_inputs(seed: int=0):
    np.random.seed(seed)
    _w = jnp.asarray

    def _rec_inputs():
        import jax
        import jax.numpy as jnp
        _gk = jax.random.key(seed)
        x = -0.0003929 + 0.9999 * jax.random.normal(jax.random.fold_in(_gk, 1), (32, 128, 32, 32), jnp.float32)
        return x
    x = _rec_inputs()

    def _L0_conv_setup():
        import jax, jax.numpy as jnp
        import numpy as np
        N, C, H, W = (32, 128, 32, 32)
        D = C // 2

        def _conv1x1(x, Wt, bt):
            return jnp.einsum('nchw,oc->nohw', x, Wt) + bt[None, :, None, None]
        key = jax.random.key(seed)
        ks = jax.random.split(key, 7)
        s = 0.05
        return {'x': jax.random.normal(ks[0], (N, C, H, W), jnp.float32), 'W_theta': jax.random.normal(ks[1], (D, C), jnp.float32) * s, 'b_theta': jax.random.normal(ks[2], (D,), jnp.float32) * s, 'W_phi': jax.random.normal(ks[3], (D, C), jnp.float32) * s, 'b_phi': jax.random.normal(ks[4], (D,), jnp.float32) * s, 'W_fuse': jax.random.normal(ks[5], (C, C), jnp.float32) * s, 'b_fuse': jax.random.normal(ks[6], (C,), jnp.float32) * s}
    _L0_conv_all = _L0_conv_setup()
    _L0_conv_in = {k: v for k, v in _L0_conv_all.items() if k in ('W_theta', 'b_theta', 'W_phi', 'b_phi', 'W_fuse', 'b_fuse')}
    del _L0_conv_all

    def _L1_conv_setup():
        import jax, jax.numpy as jnp
        import numpy as np
        NUM_GROUPS = 32
        EPS = 1e-05

        def group_norm(x, w, b):
            B, C, H, W = x.shape
            xg = x.reshape(B, NUM_GROUPS, C // NUM_GROUPS, H, W)
            mean = jnp.mean(xg, axis=(2, 3, 4), keepdims=True)
            var = jnp.var(xg, axis=(2, 3, 4), keepdims=True)
            xg = (xg - mean) * jax.lax.rsqrt(var + EPS)
            xn = xg.reshape(B, C, H, W)
            return xn * w[None, :, None, None] + b[None, :, None, None]

        def conv1x1(x, w, b):
            return jnp.einsum('bchw,oc->bohw', x, w) + b[None, :, None, None]
        key = jax.random.key(seed)
        ks = jax.random.split(key, 10)
        C = 128
        x = jax.random.normal(ks[0], (4, C, 16, 16), dtype=jnp.float32)
        s = 1.0 / np.sqrt(C)
        return {'x': x, 'gn_w': jnp.ones((C,), jnp.float32), 'gn_b': jnp.zeros((C,), jnp.float32), 'q_w': jax.random.normal(ks[1], (C, C), jnp.float32) * s, 'q_b': jax.random.normal(ks[2], (C,), jnp.float32) * 0.01, 'k_w': jax.random.normal(ks[3], (C, C), jnp.float32) * s, 'k_b': jax.random.normal(ks[4], (C,), jnp.float32) * 0.01, 'v_w': jax.random.normal(ks[5], (C, C), jnp.float32) * s, 'v_b': jax.random.normal(ks[6], (C,), jnp.float32) * 0.01, 'p_w': jax.random.normal(ks[7], (C, C), jnp.float32) * s, 'p_b': jax.random.normal(ks[8], (C,), jnp.float32) * 0.01}
    _L1_conv_all = _L1_conv_setup()
    _L1_conv_in = {k: v for k, v in _L1_conv_all.items() if k in ('gn_w', 'gn_b', 'q_w', 'q_b', 'k_w', 'k_b', 'v_w', 'v_b', 'p_w', 'p_b')}
    del _L1_conv_all
    return {'x': x, 'L0_conv_W_theta': _L0_conv_in['W_theta'], 'L0_conv_b_theta': _L0_conv_in['b_theta'], 'L0_conv_W_phi': _L0_conv_in['W_phi'], 'L0_conv_b_phi': _L0_conv_in['b_phi'], 'L0_conv_W_fuse': _L0_conv_in['W_fuse'], 'L0_conv_b_fuse': _L0_conv_in['b_fuse'], 'L1_conv_gn_w': _L1_conv_in['gn_w'], 'L1_conv_gn_b': _L1_conv_in['gn_b'], 'L1_conv_q_w': _L1_conv_in['q_w'], 'L1_conv_q_b': _L1_conv_in['q_b'], 'L1_conv_k_w': _L1_conv_in['k_w'], 'L1_conv_k_b': _L1_conv_in['k_b'], 'L1_conv_v_w': _L1_conv_in['v_w'], 'L1_conv_v_b': _L1_conv_in['v_b'], 'L1_conv_p_w': _L1_conv_in['p_w'], 'L1_conv_p_b': _L1_conv_in['p_b']}

def reference(x, L0_conv_W_theta, L0_conv_b_theta, L0_conv_W_phi, L0_conv_b_phi, L0_conv_W_fuse, L0_conv_b_fuse, L1_conv_gn_w, L1_conv_gn_b, L1_conv_q_w, L1_conv_q_b, L1_conv_k_w, L1_conv_k_b, L1_conv_v_w, L1_conv_v_b, L1_conv_p_w, L1_conv_p_b):
    import jax
    import jax.numpy as jnp

    def _L0_conv_ref(x, W_theta, b_theta, W_phi, b_phi, W_fuse, b_fuse):
        import jax, jax.numpy as jnp
        import numpy as np
        N, C, H, W = (32, 128, 32, 32)
        D = C // 2

        def _conv1x1(x, Wt, bt):
            return jnp.einsum('nchw,oc->nohw', x, Wt) + bt[None, :, None, None]
        n, c, h, w = x.shape
        theta = _conv1x1(x, W_theta, b_theta)
        phi = _conv1x1(x, W_phi, b_phi)
        d = theta.shape[1]
        hw = h * w
        t = theta.reshape(n, d, hw)
        p = phi.reshape(n, d, hw)
        g = x.reshape(n, c, hw)
        scale = 1.0 / np.sqrt(float(d))
        f = jnp.einsum('ndq,ndk->nqk', t, p) * scale
        f = jax.nn.softmax(f, axis=-1)
        attn = jnp.einsum('nqk,nck->ncq', f, g).reshape(n, c, h, w)
        return x + _conv1x1(attn, W_fuse, b_fuse)

    def _L1_conv_ref(x, gn_w, gn_b, q_w, q_b, k_w, k_b, v_w, v_b, p_w, p_b):
        import jax, jax.numpy as jnp
        import numpy as np
        NUM_GROUPS = 32
        EPS = 1e-05

        def group_norm(x, w, b):
            B, C, H, W = x.shape
            xg = x.reshape(B, NUM_GROUPS, C // NUM_GROUPS, H, W)
            mean = jnp.mean(xg, axis=(2, 3, 4), keepdims=True)
            var = jnp.var(xg, axis=(2, 3, 4), keepdims=True)
            xg = (xg - mean) * jax.lax.rsqrt(var + EPS)
            xn = xg.reshape(B, C, H, W)
            return xn * w[None, :, None, None] + b[None, :, None, None]

        def conv1x1(x, w, b):
            return jnp.einsum('bchw,oc->bohw', x, w) + b[None, :, None, None]
        h_ = group_norm(x, gn_w, gn_b)
        q = conv1x1(h_, q_w, q_b)
        k = conv1x1(h_, k_w, k_b)
        v = conv1x1(h_, v_w, v_b)
        b, c, h, w = q.shape
        n = h * w
        q = q.reshape(b, c, n).transpose(0, 2, 1)
        k = k.reshape(b, c, n)
        scores = jnp.einsum('bic,bcj->bij', q, k) * c ** (-0.5)
        attn = jax.nn.softmax(scores, axis=-1)
        v = v.reshape(b, c, n)
        h_out = jnp.einsum('bcj,bij->bci', v, attn).reshape(b, c, h, w)
        return x + conv1x1(h_out, p_w, p_b)

    def _gn(v, G=32, eps=1e-05):
        B_, C_, H_, W_ = v.shape
        g = v.reshape(B_, G, C_ // G, H_, W_)
        m = jnp.mean(g, axis=(2, 3, 4), keepdims=True)
        s = jnp.var(g, axis=(2, 3, 4), keepdims=True)
        return ((g - m) / jnp.sqrt(s + eps)).reshape(v.shape)

    def _ln_c(v, eps=1e-06):
        m = jnp.mean(v, axis=1, keepdims=True)
        s = jnp.var(v, axis=1, keepdims=True)
        return (v - m) / jnp.sqrt(s + eps)

    def _ln_t(v, eps=1e-05):
        m = jnp.mean(v, axis=-1, keepdims=True)
        s = jnp.var(v, axis=-1, keepdims=True)
        return (v - m) / jnp.sqrt(s + eps)

    def _to_tokens(v):
        B_, C_, H_, W_ = v.shape
        return v.reshape(B_, C_, H_ * W_).transpose(0, 2, 1)

    def _from_tokens(t, like):
        B_, C_, H_, W_ = like.shape
        return t.transpose(0, 2, 1).reshape(B_, C_, H_, W_)
    x = _L0_conv_ref(x, L0_conv_W_theta, L0_conv_b_theta, L0_conv_W_phi, L0_conv_b_phi, L0_conv_W_fuse, L0_conv_b_fuse)
    x = _L1_conv_ref(x, L1_conv_gn_w, L1_conv_gn_b, L1_conv_q_w, L1_conv_q_b, L1_conv_k_w, L1_conv_k_b, L1_conv_v_w, L1_conv_v_b, L1_conv_p_w, L1_conv_p_b)
    return x

_drawn_inputs = setup_inputs


def setup_inputs(seed=0):
    import zlib

    import numpy as np

    out = dict(_drawn_inputs(seed))
    spreads = {'L1_conv_gn_w': (1.0, 0.2), 'L1_conv_gn_b': (0.0, 0.1)}
    factors = {'L0_conv_W_theta': 3.288,
     'L0_conv_b_theta': 8.0,
     'L0_conv_W_phi': 3.277,
     'L0_conv_b_phi': 64.0,
     'L1_conv_q_b': 44.133,
     'L1_conv_k_b': 64.0,
     'L1_conv_v_b': 5.284,
     'L1_conv_p_b': 5.476}
    for name, (base, spread) in spreads.items():
        noise = np.random.default_rng([zlib.crc32(name.encode()), seed]).standard_normal(out[name].shape)
        drawn = base * np.exp(spread * noise) if base else spread * noise
        out[name] = jnp.asarray(drawn.astype(out[name].dtype))
    for name, factor in factors.items():
        out[name] = (out[name] * factor).astype(out[name].dtype)
    return out
```

```python
from contextlib import ExitStack

import concourse.bass as bass
from concourse import mybir

F32 = mybir.dt.float32
F32R = mybir.dt.float32r
ALU = mybir.AluOpType
ACT = mybir.ActivationFunctionType
AX = mybir.AxisListType

C = 128
D = 64
P = 128
HALF = 512
EPS = 1e-5
GROUPS = 32
SLOTS = 16
PHASE = 8
GROUP = 4
T_LAG = 3
PV_LAG = 7
OUT_LAG = 11

UNITS = {0: "gn1", 1: "gn2", 2: "v2", 3: "v3", 4: "k0", 5: "k1", 6: "q0", 7: "w0", 8: "q1",
         9: "tp0", 10: "w1", 11: "tp1", 12: "w2", 13: "w3", 14: "v0", 15: "v1"}
STAGE = {"v2": (0,), "v3": (1,), "k0": (2,), "k1": (3,), "q0": (0,), "w0": (1,), "q1": (2,), "tp0": (3, 0),
         "w1": (1,), "tp1": (2, 4), "w2": (3,), "w3": (1,), "v0": (0,), "v1": (3,)}
H_SLOT = 2
H_LO_SLOTS = (3, 4)
X_SLOT = 7
X_LO_SLOTS = (8, 10)

INS = ["x", "w_theta_t", "w_phi_t", "w_fuse_t", "q_w_t", "k_w_t", "p_w_t", "v_w", "vectors", "ident", "group_avg"]
B_TP, B_FUSE, B_Q, B_K, B_V, B_P, GN_W, GN_B = range(8)


def attention_pair(nc: bass.Bass, x, w_theta_t, w_phi_t, w_fuse_t, q_w_t, k_w_t, p_w_t, v_w, vectors,
                   ident_in, group_avg_in, y):
    NB, _, N = x.shape
    KB = N // P
    assert N == PHASE * P == 2 * HALF and NB >= 5

    def tile_at(g):
        i, s = divmod(g, SLOTS)
        return int(0 <= i < NB) if s < PHASE else int(1 <= i <= NB)

    def group_at(g):
        return int(g % GROUP == GROUP - 1 and tile_at(g))

    def unit_at(g):
        i, s = divmod(g, SLOTS)
        name = UNITS.get(s)
        if name in ("tp0", "tp1", "v0", "v1"):
            return int(-1 <= i <= NB - 2)
        if name in ("v2", "v3"):
            return int(0 <= i < NB)
        return int(name is not None and 1 <= i <= NB)

    def tp_at(g):
        return int(UNITS.get(g % SLOTS) in ("tp0", "tp1") and unit_at(g))

    def two_staged_at(g):
        return int(UNITS[g % SLOTS][0] in "tvw" and unit_at(g))

    def gn1_at(g):
        return int(UNITS.get(g % SLOTS) == "gn1" and unit_at(g))

    def split_at(g):
        own = unit_at(g - 1) if UNITS.get((g - 1) % SLOTS) not in ("gn1", "gn2") else 0
        return own + tp_at(g - 2)

    def h_at(g):
        i, s = divmod(g, SLOTS)
        return int(s == H_SLOT and 1 <= i <= NB)

    def x_at(g):
        i, s = divmod(g, SLOTS)
        return int(s == X_SLOT and -1 <= i <= NB - 2)

    def out0_at(g):
        return int(group_at(g - OUT_LAG + 3) and (g - OUT_LAG) % SLOTS < PHASE)

    def out1_at(g):
        return int(group_at(g - OUT_LAG + 3) and (g - OUT_LAG) % SLOTS >= PHASE)

    def before(what, i, s):
        if isinstance(i, int):
            return sum(what(g) for g in range(-SLOTS, SLOTS * i + s))
        at2, at3 = before(what, 2, s), before(what, 3, s)
        per = at3 - at2
        off = at2 - 2 * per
        return i * per + off if off >= 0 else i * per - (-off)

    def here(what, i, s):
        return bool(what(SLOTS * (i if isinstance(i, int) else 2) + s))

    def or_none(value):
        return max(value, 0) if isinstance(value, int) else value

    def iterations(eng, body):
        for i in (-1, 0, 1):
            body(i)
        with eng.Fori(2, NB - 1) as i:
            body(i)
        for i in (NB - 1, NB, NB + 1):
            body(i)

    with ExitStack() as ctx:
        def sb(name, shape, dt=F32):
            return ctx.enter_context(nc.sbuf_tensor(name, shape, dt))

        def ps(name, shape):
            return ctx.enter_context(nc.psum_tensor(name, shape, F32))

        def sem(name):
            return ctx.enter_context(nc.semaphore(name))

        ident = sb("ident_sb", [P, P])
        group_avg = sb("group_avg_sb", [P, P])
        vec = sb("vec", [C, 8])
        vec_ready = sb("vec_ready", [C, 3])
        neg_half = sb("neg_half", [C, 1])
        w_tp = sb("w_tp", [C, C])
        w_f = sb("w_f", [C, C])
        w_q = sb("w_q", [C, C])
        w_k = sb("w_k", [C, C])
        p_t = sb("p_t", [C, C])
        v_n = sb("v_n", [C, C])
        w_pv = sb("w_pv", [C, C])
        w_hl = {n: sb(f"w_{n}_hl", [C, 2, C], F32R) for n in ("tp", "f", "q", "k", "pv")}

        xs = sb("xs", [C, N])
        xr = sb("xr", [C, N])
        x1 = sb("x1", [C, N])
        x1_res = sb("x1_res", [C, N])
        y_sb = sb("y_sb", [C, N])
        x_hi, x_lo = sb("x_hi", [C, N], F32R), sb("x_lo", [C, N], F32R)
        h = sb("h", [C, N])
        h_hi, h_lo = sb("h_hi", [C, N], F32R), sb("h_lo", [C, N], F32R)
        stage = sb("stage", [C, 5, HALF])
        theta2 = sb("theta2", [C, N], F32R)
        phi_hi2, phi_lo2 = sb("phi_hi2", [C, N], F32R), sb("phi_lo2", [C, N], F32R)
        q_hi, q_lo = sb("q_hi", [C, N], F32R), sb("q_lo", [C, N], F32R)
        k_hi, k_lo = sb("k_hi", [C, N], F32R), sb("k_lo", [C, N], F32R)
        v_hi = [sb(f"v_hi{n}", [P, KB, C], F32R) for n in range(2)]
        v_lo = [sb(f"v_lo{n}", [P, KB, C], F32R) for n in range(2)]
        e = sb("e", [P, 4, N])
        et_hi = [sb(f"et_hi{n}", [P, KB, HALF], F32R) for n in range(2)]
        et_lo = [sb(f"et_lo{n}", [P, KB, HALF], F32R) for n in range(2)]
        neg_max, den, rden = sb("neg_max", [P, 4]), sb("den", [P, 4]), sb("rden", [P, 4])
        stats, mean_var, gmv = sb("stats", [C, 2, 6]), sb("mean_var", [C, 2]), sb("gmv", [C, 2])
        dev, dev2, gvar, gvar_eps, rstd = (sb(n, [C, 1]) for n in ("dev", "dev2", "gvar", "gvar_eps", "rstd"))
        gn_a, gn_t, gn_b = (sb(n, [C, 1]) for n in ("gn_a", "gn_t", "gn_b"))

        s_ps = ps("s_ps", [P, 2, N])
        t_ps = [ps(f"t_ps{n}", [P, HALF]) for n in range(2)]
        o_ps = ps("o_ps", [C, HALF])
        m_ps = ps("m_ps", [C, HALF])
        m_parts = m_ps[:, :].rearrange("p (b t c) -> p b t c", b=2, t=2)

        s_wload = sem("weights_loaded")
        s_const = sem("constants_set")
        s_scaled = sem("weights_scaled")
        s_wpv = sem("w_pv_product")
        s_wpv_sb = sem("w_pv_copied")
        s_whi = sem("weights_hi")
        s_weights = sem("weights_split")
        s_xs = sem("xs_loaded")
        s_xr = sem("xr_loaded")
        s_copy = [sem(f"x1_res_copied{n}") for n in range(2)]
        s_store = [sem(f"y_stored{n}") for n in range(2)]
        s_scores = sem("scores_ready")
        s_max = sem("neg_max_ready")
        s_exp = sem("exp_ready")
        s_rden = sem("rden_ready")
        s_prob = sem("prob_ready")
        s_tr = sem("transposed")
        s_thi = sem("et_hi_ready")
        s_tlo = sem("et_lo_ready")
        s_pv = sem("value_product_ready")
        s_out = sem("output_taken")
        s_unit = sem("unit_ready")
        s_evac = sem("unit_staged")
        s_evac_dve = sem("unit_staged_by_dve")
        s_split_hi = sem("split_hi")
        s_split = sem("split_done")
        s_xhi = sem("x_hi_ready")
        s_xsplit = sem("x_split")
        s_stats = sem("bn_stats_ready")
        s_mv = sem("mean_var_ready")
        s_dev, s_dev2 = sem("dev_ready"), sem("dev2_ready")
        s_veps, s_rstd, s_gna, s_gnt = (sem(n) for n in ("veps_ready", "rstd_ready", "gn_a_ready", "gn_t_ready"))
        s_gn = sem("gn_affine_ready")
        s_hhi = sem("h_hi_ready")
        s_h32 = sem("h_ready")
        s_carrier = sem("pool_wait_carrier")
        s_h = sem("h_split")

        block = ctx.enter_context(nc.Block())
        WEIGHT_LOADS = 10
        SPLITS = (("tp", w_tp), ("f", w_f), ("q", w_q), ("k", w_k), ("pv", w_pv))

        @block.sync
        def _(sp):
            for dst, src in ((w_tp[:, 0:D], w_theta_t), (w_tp[:, D:C], w_phi_t), (vec[:, :], vectors),
                             (w_f[:, :], w_fuse_t), (w_q[:, :], q_w_t), (w_k[:, :], k_w_t),
                             (p_t[:, :], p_w_t), (v_n[:, :], v_w), (ident[:, :], ident_in),
                             (group_avg[:, :], group_avg_in)):
                sp.dma_start(dst, src).then_inc(s_wload, 16)

            def batch(t, b):
                return t[b] if isinstance(b, int) else t[bass.ds(b, 1)].rearrange("a c n -> c (a n)")

            def body(i):
                if here(x_at, i, X_SLOT):
                    sp.wait_ge(s_xsplit, 2 * before(x_at, i, 0))
                    sp.dma_start(xs[:, :], batch(x, i + 1)).then_inc(s_xs, 16)
                if here(out0_at, i, OUT_LAG):
                    sp.wait_ge(s_out, before(group_at, i, -PHASE))
                    sp.dma_start(xr[:, :], batch(x, i)).then_inc(s_xr, 16)
                for half, s in ((0, OUT_LAG - PHASE), (1, OUT_LAG - PHASE + GROUP)):
                    cols = slice(half * HALF, (half + 1) * HALF)
                    sp.wait_ge(s_out, before(group_at, i, s + 1 - OUT_LAG + 3))
                    if here(out1_at, i, s):
                        sp.dma_start(batch(y, i - 2)[:, cols], y_sb[:, cols]).then_inc(s_store[half], 16)
                    if here(h_at, i, H_SLOT):
                        sp.dma_start(x1_res[:, cols], x1[:, cols]).then_inc(s_copy[half], 16)

            iterations(sp, body)
            for half in range(2):
                sp.wait_ge(s_store[half], 16 * NB)

        @block.tensor
        def _(pe):
            pe.wait_ge(s_wload, 16 * WEIGHT_LOADS)
            pe.matmul(m_ps[:, 0:C], v_n[:, :], p_t[:, :], start=True, stop=True)
            pe.matmul(m_ps[:, C:C + 1], p_t[:, :], vec[:, B_V:B_V + 1], start=True, stop=True).then_inc(s_wpv, 1)
            pe.wait_ge(s_weights, len(SPLITS))

            def product(out, terms, start=True, stop=True):
                for n, (lhs_t, rhs) in enumerate(terms):
                    mm = pe.matmul(out, lhs_t, rhs, start=start and n == 0, stop=stop and n == len(terms) - 1)
                return mm

            def transposes(i, s, half):
                if not here(tile_at, i, s - T_LAG):
                    return
                n = before(tile_at, i, s - T_LAG)
                if half == 0:
                    pe.wait_ge(s_prob, n + 1)
                pe.wait_ge(s_tlo, or_none(2 * n - 1 + half))
                for b in range(GROUP):
                    kb = GROUP * half + b
                    mm = pe.transpose(t_ps[half][:, b * P:(b + 1) * P],
                                      e[:, (s - T_LAG) % 4, kb * P:(kb + 1) * P], ident[:, :])
                mm.then_inc(s_tr, 1)

            def scores(i, s, half):
                if not here(tile_at, i, s):
                    return
                n = before(tile_at, i, s)
                if half == 0:
                    pe.wait_ge(s_exp, or_none(n - 1))
                    if s == 0:
                        pe.wait_ge(s_split, before(split_at, i, -3) + 1)
                    if s == PHASE:
                        pe.wait_ge(s_split, before(split_at, i, 8))
                    if s == PHASE + GROUP:
                        pe.wait_ge(s_split, before(split_at, i, 10))
                out = s_ps[:, s % 2, half * HALF:(half + 1) * HALF]
                t = s % PHASE
                qs, ks = slice(t * P, (t + 1) * P), slice(half * HALF, (half + 1) * HALF)
                if s < PHASE:
                    mm = product(out, [(theta2[:, qs], phi_hi2[:, ks]), (theta2[:, qs], phi_lo2[:, ks])])
                else:
                    mm = product(out, [(q_hi[:, qs], k_hi[:, ks]), (q_hi[:, qs], k_lo[:, ks]),
                                       (q_lo[:, qs], k_hi[:, ks])])
                if half == 1:
                    mm.then_inc(s_scores, 1)

            def values(i, s):
                quarter = (s - PV_LAG) % GROUP
                first = s - PV_LAG - quarter
                if not here(tile_at, i, first):
                    return
                layer = int(first % SLOTS >= PHASE)
                if quarter == 0:
                    pe.wait_ge(s_tlo, 2 * before(tile_at, i, first + GROUP))
                    if s == PV_LAG:
                        pe.wait_ge(s_split, before(split_at, i, 5))
                    if s == PV_LAG + PHASE:
                        pe.wait_ge(s_split, before(split_at, i, 15))
                    pe.wait_ge(s_out, before(group_at, i, first))
                g = first // GROUP % 2
                for kb in (2 * quarter, 2 * quarter + 1):
                    mm = product(o_ps[:, :], [(v_hi[layer][:, kb, :], et_hi[g][:, kb, :]),
                                              (v_lo[layer][:, kb, :], et_hi[g][:, kb, :]),
                                              (v_hi[layer][:, kb, :], et_lo[g][:, kb, :])],
                                 start=kb == 0, stop=kb == KB - 1)
                if quarter == 3:
                    mm.then_inc(s_pv, 1)

            def unit(i, s):
                if not here(unit_at, i, s):
                    return
                name = UNITS[s]
                pe.wait_ge(s_evac, before(unit_at, i, s))
                pe.wait_ge(s_evac_dve, before(two_staged_at, i, s))
                if name == "gn1":
                    pe.wait_ge(s_mv, before(gn1_at, i, s) + 1)
                    mm = pe.matmul(m_ps[:, 0:2], group_avg[:, :], mean_var[:, :], start=True, stop=True)
                elif name == "gn2":
                    pe.wait_ge(s_dev2, before(gn1_at, i, s))
                    mm = pe.matmul(m_ps[:, 0:1], group_avg[:, :], dev2[:, :], start=True, stop=True)
                else:
                    part = int(name[-1])
                    half = part // 2 if name[0] in "vw" else part
                    if name[0] in "tv":
                        pe.wait_ge(s_xsplit, 2 * before(x_at, i, s) - 1 + half)
                        hi, lo, w = x_hi, x_lo, w_hl["tp" if name[0] == "t" else "f"]
                    else:
                        pe.wait_ge(s_h, 2 * before(h_at, i, s) - 1 + half)
                        hi, lo, w = h_hi, h_lo, w_hl[{"k": "k", "q": "q", "w": "pv"}[name[0]]]
                    if name[0] in "vw":
                        for b in range(2):
                            px = slice((2 * part + b) * P, (2 * part + b + 1) * P)
                            pe.matmul(m_ps[:, 2 * b * C:2 * (b + 1) * C], hi[:, px],
                                      w[:, :, :].rearrange("p a c -> p (a c)"), start=True, stop=False)
                            mm = pe.matmul(m_ps[:, 2 * b * C:(2 * b + 1) * C], lo[:, px], w[:, 0, :],
                                           start=False, stop=True)
                    else:
                        px = slice(half * HALF, (half + 1) * HALF)
                        mm = product(m_ps[:, :], [(w[:, 0, :], hi[:, px]), (w[:, 0, :], lo[:, px]),
                                                  (w[:, 1, :], hi[:, px])])
                mm.then_inc(s_unit, 1)

            def body(i):
                for s in range(SLOTS):
                    transposes(i, s, 0)
                    scores(i, s, 0)
                    transposes(i, s, 1)
                    scores(i, s, 1)
                    unit(i, s)
                    values(i, s)

            iterations(pe, body)

        @block.scalar
        def _(act):
            act.wait_ge(s_wload, 16 * WEIGHT_LOADS)
            nc.scalar.activation(w_tp[:, 0:D], w_tp[:, 0:D], ACT.Copy, scale=D ** -0.5).then_inc(s_scaled, 1)
            nc.scalar.activation(w_q[:, :], w_q[:, :], ACT.Copy, scale=C ** -0.5).then_inc(s_scaled, 1)
            nc.scalar.activation(vec_ready[0:D, 0:1], vec[0:D, B_TP:B_TP + 1], ACT.Copy,
                                 scale=D ** -0.5).then_inc(s_scaled, 1)
            nc.scalar.activation(vec_ready[D:C, 0:1], vec[D:C, B_TP:B_TP + 1], ACT.Copy).then_inc(s_scaled, 1)
            nc.scalar.activation(vec_ready[:, 1:2], vec[:, B_Q:B_Q + 1], ACT.Copy,
                                 scale=C ** -0.5).then_inc(s_scaled, 1)
            act.wait_ge(s_wpv, 1)
            nc.scalar.activation(w_pv[:, :], m_ps[:, 0:C], ACT.Copy).then_inc(s_wpv_sb, 1)
            nc.scalar.activation(vec_ready[:, 2:3], m_ps[:, C:C + 1], ACT.Identity,
                                 bias=vec[:, B_P:B_P + 1]).then_inc(s_scaled, 1)
            act.wait_ge(s_scaled, 6)

            def take_hi(i, s, half):
                t = s - T_LAG
                if not here(tile_at, i, t):
                    return
                if half == 0 and t % GROUP == 0:
                    act.wait_ge(s_pv, or_none(before(group_at, i, t) - 1))
                act.wait_ge(s_tr, 2 * before(tile_at, i, t) + 1 + half)
                cols = slice(t % GROUP * P, (t % GROUP + 1) * P)
                nc.scalar.activation(et_hi[t // GROUP % 2][:, GROUP * half:GROUP * (half + 1), cols],
                                     t_ps[half][:, :].rearrange("k (b q) -> k b q", b=GROUP),
                                     ACT.Copy).then_inc(s_thi, 1)

            def stage_unit(i, s):
                if not here(unit_at, i, s):
                    return
                name = UNITS[s]
                act.wait_ge(s_unit, before(unit_at, i, s) + 1)
                if name == "gn1":
                    nc.scalar.activation(gmv[:, :], m_ps[:, 0:2], ACT.Copy).then_inc(s_evac, 1)
                    return
                if name == "gn2":
                    nc.scalar.activation(gvar[:, :], m_ps[:, 0:1], ACT.Identity,
                                         bias=gmv[:, 1:2]).then_inc(s_evac, 1)
                    return
                act.wait_ge(s_split, before(split_at, i, s - 1))
                dst = stage[:, STAGE[name][0], :]
                if name[0] == "t":
                    nc.scalar.activation(dst[0:D, :], m_ps[0:D, :], ACT.Identity, bias=vec_ready[0:D, 0:1])
                    nc.scalar.activation(dst[D:C, :], m_ps[0:D, :], ACT.Identity,
                                         bias=vec_ready[0:D, 0:1]).then_inc(s_evac, 1)
                elif name[0] in "vw":
                    nc.scalar.activation(dst[:, 0:2 * C].rearrange("p (b c) -> p b c", b=2),
                                         m_parts[:, :, 1, :], ACT.Copy).then_inc(s_evac, 1)
                else:
                    bias = vec_ready[:, 1:2] if name[0] == "q" else vec[:, B_K:B_K + 1]
                    nc.scalar.activation(dst, m_ps[:, :], ACT.Identity, bias=bias).then_inc(s_evac, 1)

            def inputs_hi(i, s):
                if here(h_at, i, s):
                    act.wait_ge(s_gn, before(h_at, i, s) + 1)
                    act.wait_ge(s_unit, before(unit_at, i, 0))
                    nc.scalar.activation(h_hi[:, :], x1[:, :], ACT.Identity, scale=gn_a[:, 0:1],
                                         bias=gn_b[:, 0:1]).then_inc(s_hhi, 1)
                if here(x_at, i, s):
                    act.wait_ge(s_xs, 16 * (before(x_at, i, s) + 1))
                    act.wait_ge(s_unit, before(unit_at, i, 4))
                    nc.scalar.activation(x_hi[:, :], xs[:, :], ACT.Copy).then_inc(s_xhi, 1)

            def exponentials(i, s):
                s = s - 1
                if not here(tile_at, i, s):
                    return
                n = before(tile_at, i, s)
                act.wait_ge(s_max, n + 1)
                act.wait_ge(s_tr, or_none(2 * n - 6))
                nc.scalar.activation(e[:, s % 4, :], s_ps[:, s % 2, :], ACT.Exp, bias=neg_max[:, s % 4:s % 4 + 1],
                                     accum_out=den[:, s % 4:s % 4 + 1]).then_inc(s_exp, 1)

            def body(i):
                for s in range(SLOTS):
                    take_hi(i, s, 0)
                    take_hi(i, s, 1)
                    exponentials(i, s)
                    stage_unit(i, s)
                    inputs_hi(i, s)

            iterations(act, body)

        @block.vector
        def _(dve):
            for n, (name, w) in enumerate(SPLITS):
                dve.wait_ge(*{"tp": (s_scaled, 1), "f": (s_wload, 16 * WEIGHT_LOADS), "q": (s_scaled, 2),
                              "k": (s_wload, 16 * WEIGHT_LOADS), "pv": (s_wpv_sb, 1)}[name])
                nc.vector.tensor_copy(w_hl[name][:, 0, :], w[:, :]).then_inc(s_whi, 1)
                dve.wait_ge(s_whi, n + 1)
                nc.vector.tensor_tensor(w_hl[name][:, 1, :], w[:, :], w_hl[name][:, 0, :].bitcast(F32),
                                        ALU.subtract).then_inc(s_weights, 1)
            dve.wait_ge(s_scaled, 6)

            def reciprocal(i, s):
                if not here(tile_at, i, s - 2):
                    return
                dve.wait_ge(s_exp, before(tile_at, i, s - 2) + 1)
                c = (s - 2) % 4
                nc.vector.reciprocal(rden[:, c:c + 1], den[:, c:c + 1]).then_inc(s_rden, 1)

            def take_lo(i, s, half):
                t = s - T_LAG
                if not here(tile_at, i, t):
                    return
                dve.wait_ge(s_thi, 2 * before(tile_at, i, t) + 1 + half)
                blocks, cols = slice(GROUP * half, GROUP * (half + 1)), slice(t % GROUP * P, (t % GROUP + 1) * P)
                g = t // GROUP % 2
                nc.vector.tensor_tensor(et_lo[g][:, blocks, cols],
                                        t_ps[half][:, :].rearrange("k (b q) -> k b q", b=GROUP),
                                        et_hi[g][:, blocks, cols].bitcast(F32), ALU.subtract).then_inc(s_tlo, 1)

            def maxima(i, s):
                s = s - 1
                if not here(tile_at, i, s):
                    return
                dve.wait_ge(s_scores, before(tile_at, i, s) + 1)
                nc.vector.tensor_reduce(neg_max[:, s % 4:s % 4 + 1], s_ps[:, s % 2, :], AX.X, ALU.max,
                                        negate=True).then_inc(s_max, 1)

            def outputs(i, s):
                first = s - OUT_LAG
                half = first // GROUP % 2
                cols = slice(half * HALF, (half + 1) * HALF)
                if here(out0_at, i, s):
                    dve.wait_ge(s_pv, before(group_at, i, first) + 1)
                    dve.wait_ge(s_xr, i * 16 + 16)
                    dve.wait_ge(s_h, 2 * before(h_at, i, s))
                    dve.wait_ge(s_hhi, before(h_at, i, s))
                    dve.wait_ge(s_copy[half], 16 * before(h_at, i, s))
                    nc.vector.scalar_tensor_tensor(out=x1[:, cols], in0=o_ps[:, :], scalar=vec[:, B_FUSE:B_FUSE + 1],
                                                   in1=xr[:, cols], op0=ALU.add, op1=ALU.add).then_inc(s_out, 1)
                if here(out1_at, i, s):
                    dve.wait_ge(s_pv, before(group_at, i, first) + 1)
                    n = before(lambda g: out1_at(g) and (g - OUT_LAG) // GROUP % 2 == half, i, s)
                    dve.wait_ge(s_copy[half], 16 * (n + 1))
                    dve.wait_ge(s_store[half], 16 * n)
                    nc.vector.scalar_tensor_tensor(out=y_sb[:, cols], in0=o_ps[:, :], scalar=vec_ready[:, 2:3],
                                                   in1=x1_res[:, cols], op0=ALU.add, op1=ALU.add).then_inc(s_out, 1)

            def statistics(i, s):
                if not here(out0_at, i, s):
                    return
                half = (s - OUT_LAG) // GROUP % 2
                n = before(out0_at, i, s)
                dve.wait_ge(s_out, before(group_at, i, s - OUT_LAG) + 1)
                nc.vector.bn_stats(stats[:, half, :], x1[:, half * HALF:(half + 1) * HALF]).then_inc(s_stats, 1)
                if half == 1:
                    dve.wait_ge(s_stats, n + 1)

            def aggregate(i, s):
                if here(out0_at, i, s) and (s - OUT_LAG) // GROUP % 2 == 1:
                    nc.vector.bn_aggr(mean_var[:, :], stats[:, :, :].rearrange("p a b -> p (a b)")).then_inc(s_mv, 1)

            def stage_unit(i, s):
                if not here(two_staged_at, i, s):
                    return
                name = UNITS[s]
                if name[0] in "vw":
                    dve.wait_ge(s_evac, before(unit_at, i, s) + 1)
                    part, total = (stage[:, STAGE[name][0], n:n + 2 * C].rearrange("p (b c) -> p b c", b=2)
                                   for n in (0, 2 * C))
                    nc.vector.tensor_tensor(total, m_parts[:, :, 0, :], part, ALU.add).then_inc(s_evac_dve, 1)
                    return
                dve.wait_ge(s_unit, before(unit_at, i, s) + 1)
                dve.wait_ge(s_split, before(split_at, i, s - 1))
                dst = stage[:, STAGE[name][1], :]
                nc.vector.tensor_scalar(dst[D:C, :], m_ps[D:C, :], vec_ready[D:C, 0:1], None, ALU.add)
                nc.vector.tensor_scalar(dst[0:D, :], m_ps[D:C, :], vec_ready[D:C, 0:1], None,
                                        ALU.add).then_inc(s_evac_dve, 1)

            def body(i):
                for s in range(SLOTS):
                    reciprocal(i, s)
                    outputs(i, s)
                    statistics(i, s)
                    maxima(i, s)
                    aggregate(i, s)
                    take_lo(i, s, 0)
                    take_lo(i, s, 1)
                    stage_unit(i, s)

            iterations(dve, body)

        @block.gpsimd
        def _(pool):
            nc.gpsimd.memset(neg_half[:, :], -0.5).then_inc(s_const, 1)
            pool.wait_ge(s_const, 1)
            pool.wait_ge(s_wload, 16 * WEIGHT_LOADS)

            def scaled(*args):
                pool.sem_inc(s_carrier)
                return nc.gpsimd.tensor_scalar(*args)

            def normalise(i, s):
                if not here(tile_at, i, s - 2):
                    return
                pool.wait_ge(s_rden, before(tile_at, i, s - 2) + 1)
                c = (s - 2) % 4
                scaled(e[:, c, :], e[:, c, :], rden[:, c:c + 1], 1.0, ALU.mult,
                                        ALU.mult).then_inc(s_prob, 1)

            def rounded(out, in_, sem):
                scaled(out, in_, 1.0, 1.0, ALU.mult, ALU.mult).then_inc(sem, 1)

            def rest(out, in_, hi, sem):
                nc.gpsimd.tensor_tensor(out, in_, hi.bitcast(F32), ALU.subtract).then_inc(sem, 1)

            def group_norm(i, s):
                if UNITS.get(s) == "gn1" and here(unit_at, i, s):
                    n = before(h_at, i, 0)
                    pool.wait_ge(s_evac, before(unit_at, i, s) + 1)
                    nc.gpsimd.tensor_tensor(dev[:, :], mean_var[:, 0:1], gmv[:, 0:1], ALU.subtract).then_inc(s_dev, 1)
                    pool.wait_ge(s_dev, n + 1)
                    nc.gpsimd.tensor_tensor(dev2[:, :], dev[:, :], dev[:, :], ALU.mult).then_inc(s_dev2, 1)
                if UNITS.get(s) == "gn2" and here(unit_at, i, s):
                    n = before(h_at, i, 0)
                    pool.wait_ge(s_evac, before(unit_at, i, s) + 1)
                    scaled(gvar_eps[:, :], gvar[:, :], EPS, 1.0, ALU.add, ALU.mult).then_inc(s_veps, 1)
                    pool.wait_ge(s_veps, n + 1)
                    nc.gpsimd.tensor_tensor(rstd[:, :], gvar_eps[:, :], neg_half[:, :], ALU.pow).then_inc(s_rstd, 1)
                    pool.wait_ge(s_rstd, n + 1)
                    nc.gpsimd.tensor_tensor(gn_a[:, :], rstd[:, :], vec[:, GN_W:GN_W + 1], ALU.mult).then_inc(s_gna, 1)
                    pool.wait_ge(s_gna, n + 1)
                    nc.gpsimd.tensor_tensor(gn_t[:, :], gmv[:, 0:1], gn_a[:, :], ALU.mult).then_inc(s_gnt, 1)
                    pool.wait_ge(s_gnt, n + 1)
                    nc.gpsimd.tensor_tensor(gn_b[:, :], vec[:, GN_B:GN_B + 1], gn_t[:, :], ALU.subtract).then_inc(s_gn, 1)

            def inputs_lo(i, s):
                if here(h_at, i, s):
                    n = before(h_at, i, s)
                    pool.wait_ge(s_gn, n + 1)
                    scaled(h[:, :], x1[:, :], gn_a[:, 0:1], gn_b[:, 0:1], ALU.mult,
                                            ALU.add).then_inc(s_h32, 1)
                if s in H_LO_SLOTS and here(h_at, i, H_SLOT):
                    half = H_LO_SLOTS.index(s)
                    cols = slice(half * HALF, (half + 1) * HALF)
                    pool.wait_ge(s_h32, before(h_at, i, s))
                    pool.wait_ge(s_hhi, before(h_at, i, s))
                    rest(h_lo[:, cols], h[:, cols], h_hi[:, cols], s_h)
                if s in X_LO_SLOTS and here(x_at, i, X_SLOT):
                    half = X_LO_SLOTS.index(s)
                    cols = slice(half * HALF, (half + 1) * HALF)
                    pool.wait_ge(s_xhi, before(x_at, i, s))
                    rest(x_lo[:, cols], xs[:, cols], x_hi[:, cols], s_xsplit)

            def split_phi(i, s):
                if not here(tp_at, i, s - 2):
                    return
                name = UNITS[(s - 2) % SLOTS]
                cols = slice(int(name[-1]) * HALF, (int(name[-1]) + 1) * HALF)
                src = stage[:, STAGE[name][1], :]
                pool.wait_ge(s_evac_dve, before(two_staged_at, i, s - 2) + 1)
                pool.wait_ge(s_scores, before(tile_at, i, PHASE))
                rounded(phi_hi2[:, cols], src, s_split_hi)
                pool.wait_ge(s_split_hi, before(split_at, i, s) + 1)
                rest(phi_lo2[:, cols], src, phi_hi2[:, cols], s_split)

            def split(i, s):
                name = UNITS.get((s - 1) % SLOTS)
                if name in (None, "gn1", "gn2") or not here(unit_at, i, s - 1):
                    return
                half = int(name[-1])
                cols = slice(half * HALF, (half + 1) * HALF)
                src = stage[:, STAGE[name][0], :]
                done = before(split_at, i, s) + here(tp_at, i, s - 2)
                pool.wait_ge(s_evac, before(unit_at, i, s - 1) + 1)
                if name[0] == "t":
                    pool.wait_ge(s_scores, before(tile_at, i, PHASE))
                    rounded(theta2[:, cols], src, s_split_hi)
                    pool.wait_ge(s_split_hi, done + 1)
                    rest(theta2[D:C, cols], src[D:C, :], theta2[D:C, cols], s_split)
                    pool.wait_ge(s_split, done + 1)
                    return
                if name[0] in "vw":
                    pool.wait_ge(s_evac_dve, before(two_staged_at, i, s - 1) + 1)
                    pool.wait_ge(s_pv, before(group_at, i, 0) if name[0] == "w"
                                 else before(group_at, i, PHASE if s > PHASE else -PHASE))
                    part = int(name[-1])
                    values = (v_hi[1], v_lo[1]) if name[0] == "w" else (v_hi[0], v_lo[0])
                    hi, lo = (v[:, 2 * part:2 * (part + 1), :] for v in values)
                    src = src[:, 2 * C:4 * C].rearrange("p (b c) -> p b c", b=2)
                else:
                    pool.wait_ge(s_scores, before(tile_at, i, 0))
                    hi, lo = (q_hi[:, cols], q_lo[:, cols]) if name[0] == "q" else (k_hi[:, cols], k_lo[:, cols])
                rounded(hi, src, s_split_hi)
                pool.wait_ge(s_split_hi, done + 1)
                rest(lo, src, hi, s_split)

            def body(i):
                for s in range(SLOTS):
                    normalise(i, s)
                    inputs_lo(i, s)
                    split_phi(i, s)
                    split(i, s)
                    group_norm(i, s)

            iterations(pool, body)


def kernel(x, L0_conv_W_theta, L0_conv_b_theta, L0_conv_W_phi, L0_conv_b_phi, L0_conv_W_fuse, L0_conv_b_fuse,
           L1_conv_gn_w, L1_conv_gn_b, L1_conv_q_w, L1_conv_q_b, L1_conv_k_w, L1_conv_k_b, L1_conv_v_w,
           L1_conv_v_b, L1_conv_p_w, L1_conv_p_b):
    import numpy as np
    import concourse.bacc as bacc
    from concourse.bass_utils import run_bass_kernel_spmd

    x = np.asarray(x)
    nb, c, hh, ww = x.shape
    per_group = c // GROUPS
    t = lambda w: np.ascontiguousarray(np.asarray(w).T)
    arrays = {
        "x": np.ascontiguousarray(x.reshape(nb, c, hh * ww)),
        "w_theta_t": t(L0_conv_W_theta), "w_phi_t": t(L0_conv_W_phi), "w_fuse_t": t(L0_conv_W_fuse),
        "q_w_t": t(L1_conv_q_w), "k_w_t": t(L1_conv_k_w), "p_w_t": t(L1_conv_p_w),
        "v_w": np.ascontiguousarray(L1_conv_v_w),
        "vectors": np.ascontiguousarray(np.stack(
            [np.concatenate([np.asarray(L0_conv_b_theta), np.asarray(L0_conv_b_phi)])]
            + [np.asarray(v) for v in (L0_conv_b_fuse, L1_conv_q_b, L1_conv_k_b, L1_conv_v_b, L1_conv_p_b,
                                       L1_conv_gn_w, L1_conv_gn_b)], axis=1)),
        "ident": np.eye(c, dtype=np.float32),
        "group_avg": np.kron(np.eye(GROUPS), np.full((per_group, per_group), 1 / per_group)).astype(np.float32),
    }
    nc = bacc.Bacc("TRN2", target_bir_lowering=False, num_devices=1)
    args = [nc.dram_tensor(f"in_{n}", arrays[n].shape, F32, kind="ExternalInput").ap() for n in INS]
    out = nc.dram_tensor("out_y", (nb, c, hh * ww), F32, kind="ExternalOutput").ap()
    attention_pair(nc, *args, out)
    r = run_bass_kernel_spmd(nc, [{f"in_{n}": arrays[n] for n in INS}], core_ids=[0])
    return np.asarray(r.results[0]["out_y"]).reshape(nb, c, hh, ww)
```

```python
from contextlib import ExitStack

import concourse.bass as bass
from concourse import mybir

F32 = mybir.dt.float32
F32R = mybir.dt.float32r
ALU = mybir.AluOpType
ACT = mybir.ActivationFunctionType
AX = mybir.AxisListType

C = 128
D = 64
P = 128
HALF = 512
EPS = 1e-5
GROUPS = 32
SLOTS = 16
PHASE = 8
GROUP = 4
T_LAG = 3
PV_LAG = 7
OUT_LAG = 11

UNITS = {0: "gn1", 1: "gn2", 2: "v2", 3: "v3", 4: "k0", 5: "k1", 6: "q0", 7: "w0", 8: "q1",
         9: "tp0", 10: "w1", 11: "tp1", 12: "w2", 13: "w3", 14: "v0", 15: "v1"}
STAGES = 4
STAGE = {name: n % STAGES for n, name in enumerate(UNITS[s] for s in range(SLOTS) if UNITS[s][0] in "vw")}
H_SLOT = 2
H_LO_SLOTS = (3, 4)
X_SLOT = 7
X_LO_SLOTS = (8, 10)

INS = ["x", "w_theta_t", "w_phi_t", "w_fuse_t", "q_w_t", "k_w_t", "p_w_t", "v_w", "vectors", "ident", "group_avg"]
B_TP, B_FUSE, B_Q, B_K, B_V, B_P, GN_W, GN_B = range(8)


def attention_pair(nc: bass.Bass, x, w_theta_t, w_phi_t, w_fuse_t, q_w_t, k_w_t, p_w_t, v_w, vectors,
                   ident_in, group_avg_in, y):
    NB, _, N = x.shape
    KB = N // P
    assert N == PHASE * P == 2 * HALF and NB >= 5

    def tile_at(g):
        i, s = divmod(g, SLOTS)
        return int(0 <= i < NB) if s < PHASE else int(1 <= i <= NB)

    def group_at(g):
        return int(g % GROUP == GROUP - 1 and tile_at(g))

    def unit_at(g):
        i, s = divmod(g, SLOTS)
        name = UNITS.get(s)
        if name in ("tp0", "tp1", "v0", "v1"):
            return int(-1 <= i <= NB - 2)
        if name in ("v2", "v3"):
            return int(0 <= i < NB)
        return int(name is not None and 1 <= i <= NB)

    def tp_at(g):
        return int(UNITS.get(g % SLOTS) in ("tp0", "tp1") and unit_at(g))

    def direct_at(g):
        return int(UNITS[g % SLOTS][0] in "tqk" and unit_at(g))

    def values_at(g):
        return int(UNITS[g % SLOTS][0] in "vw" and unit_at(g))

    def gn1_at(g):
        return int(UNITS.get(g % SLOTS) == "gn1" and unit_at(g))

    def h_at(g):
        i, s = divmod(g, SLOTS)
        return int(s == H_SLOT and 1 <= i <= NB)

    def x_at(g):
        i, s = divmod(g, SLOTS)
        return int(s == X_SLOT and -1 <= i <= NB - 2)

    def out0_at(g):
        return int(group_at(g - OUT_LAG + 3) and (g - OUT_LAG) % SLOTS < PHASE)

    def out1_at(g):
        return int(group_at(g - OUT_LAG + 3) and (g - OUT_LAG) % SLOTS >= PHASE)

    def before(what, i, s):
        if isinstance(i, int):
            return sum(what(g) for g in range(-SLOTS, SLOTS * i + s))
        at2, at3 = before(what, 2, s), before(what, 3, s)
        per = at3 - at2
        off = at2 - 2 * per
        return i * per + off if off >= 0 else i * per - (-off)

    def here(what, i, s):
        return bool(what(SLOTS * (i if isinstance(i, int) else 2) + s))

    def or_none(value):
        return max(value, 0) if isinstance(value, int) else value

    def iterations(eng, body, first):
        for i in range(first, 2):
            body(i)
        with eng.Fori(2, NB - 1) as i:
            body(i)
        for i in (NB - 1, NB, NB + 1):
            body(i)

    with ExitStack() as ctx:
        def sb(name, shape, dt=F32):
            return ctx.enter_context(nc.sbuf_tensor(name, shape, dt))

        def ps(name, shape):
            return ctx.enter_context(nc.psum_tensor(name, shape, F32))

        def sem(name):
            return ctx.enter_context(nc.semaphore(name))

        ident = sb("ident_sb", [P, P])
        group_avg = sb("group_avg_sb", [P, P])
        vec = sb("vec", [C, 8])
        vec_ready = sb("vec_ready", [C, 3])
        neg_half = sb("neg_half", [C, 1])
        w_tp = sb("w_tp", [C, C])
        w_f = sb("w_f", [C, C])
        w_q = sb("w_q", [C, C])
        w_k = sb("w_k", [C, C])
        p_t = sb("p_t", [C, C])
        v_n = sb("v_n", [C, C])
        w_pv = sb("w_pv", [C, C])
        w_hl = {n: sb(f"w_{n}_hl", [C, 2, C], F32R) for n in ("tp", "f", "q", "k", "pv")}

        xs = sb("xs", [C, N])
        xr = sb("xr", [C, N])
        x1 = sb("x1", [C, N])
        x1_res = sb("x1_res", [C, N])
        y_sb = sb("y_sb", [C, N])
        x_hi, x_lo = sb("x_hi", [C, N], F32R), sb("x_lo", [C, N], F32R)
        h = sb("h", [C, N])
        h_hi, h_lo = sb("h_hi", [C, N], F32R), sb("h_lo", [C, N], F32R)
        stage = sb("stage", [P, STAGES, 2, 2, C])
        theta2 = sb("theta2", [C, N], F32R)
        phi2 = sb("phi2", [C, 2, N], F32R)
        q_hi, q_lo = sb("q_hi", [C, N], F32R), sb("q_lo", [C, N], F32R)
        k_hi, k_lo = sb("k_hi", [C, N], F32R), sb("k_lo", [C, N], F32R)
        v_hi = [sb(f"v_hi{n}", [P, KB, C], F32R) for n in range(2)]
        v_lo = [sb(f"v_lo{n}", [P, KB, C], F32R) for n in range(2)]
        e = sb("e", [P, 4, N])
        et_hi = [sb(f"et_hi{n}", [P, KB, HALF], F32R) for n in range(2)]
        et_lo = [sb(f"et_lo{n}", [P, KB, HALF], F32R) for n in range(2)]
        neg_max, den, rden = sb("neg_max", [P, 4]), sb("den", [P, 4]), sb("rden", [P, 4])
        stats, mean_var, gmv = sb("stats", [C, 2, 6]), sb("mean_var", [C, 2]), sb("gmv", [C, 2])
        dev, dev2, gvar, gvar_eps, rstd = (sb(n, [C, 1]) for n in ("dev", "dev2", "gvar", "gvar_eps", "rstd"))
        gn_a, gn_t, gn_b = (sb(n, [C, 1]) for n in ("gn_a", "gn_t", "gn_b"))

        s_ps = ps("s_ps", [P, 2, N])
        t_ps = [ps(f"t_ps{n}", [P, HALF]) for n in range(2)]
        o_ps = ps("o_ps", [C, HALF])
        m_ps = ps("m_ps", [C, HALF])

        def first_units(i):
            return isinstance(i, int) and i == -1

        def bank(i, s):
            return o_ps if first_units(i) and UNITS[s] in ("tp1", "v1") else m_ps

        s_wload0 = sem("layer0_weights_loaded")
        s_wload = sem("other_weights_loaded")
        s_const = sem("constants_set")
        s_scaled = sem("weights_scaled")
        s_wpv = sem("w_pv_product")
        s_wpv_sb = sem("w_pv_copied")
        s_whi = sem("weights_hi")
        s_weights = sem("weights_split")
        s_xs = sem("xs_loaded")
        s_xr = sem("xr_loaded")
        s_copy = [sem(f"x1_res_copied{n}") for n in range(2)]
        s_store = [sem(f"y_stored{n}") for n in range(2)]
        s_scores = sem("scores_ready")
        s_max = sem("neg_max_ready")
        s_exp = sem("exp_ready")
        s_rden = sem("rden_ready")
        s_prob = sem("prob_ready")
        s_tr = sem("transposed")
        s_thi = sem("et_hi_ready")
        s_tlo = sem("et_lo_ready")
        s_pv = sem("value_product_ready")
        s_out = sem("output_taken")
        s_unit = sem("unit_ready")
        s_evac = sem("unit_taken_by_act")
        s_theta = sem("theta_hi_ready")
        s_direct = sem("unit_hi_lo_ready")
        s_phi = sem("phi_twice")
        s_sum = sem("values_summed")
        s_split_hi = sem("values_hi")
        s_split = sem("values_split")
        s_xhi = sem("x_hi_ready")
        s_xsplit = sem("x_split")
        s_stats = sem("bn_stats_ready")
        s_mv = sem("mean_var_ready")
        s_dev, s_dev2 = sem("dev_ready"), sem("dev2_ready")
        s_veps, s_rstd, s_gna, s_gnt = (sem(n) for n in ("veps_ready", "rstd_ready", "gn_a_ready", "gn_t_ready"))
        s_gn = sem("gn_affine_ready")
        s_hhi = sem("h_hi_ready")
        s_h32 = sem("h_ready")
        s_carrier = sem("pool_wait_carrier")
        s_h = sem("h_split")

        block = ctx.enter_context(nc.Block())
        LOADS0 = ((w_tp[:, 0:D], w_theta_t), (w_tp[:, D:C], w_phi_t), (vec[:, :], vectors), (w_f[:, :], w_fuse_t))
        LOADS = ((ident[:, :], ident_in), (p_t[:, :], p_w_t), (v_n[:, :], v_w), (w_q[:, :], q_w_t),
                 (w_k[:, :], k_w_t), (group_avg[:, :], group_avg_in))

        SPLITS = (("tp", w_tp), ("f", w_f), ("q", w_q), ("k", w_k), ("pv", w_pv))

        @block.sync
        def _(sp):
            sp.dma_start(xs[:, :], x[0]).then_inc(s_xs, 16)
            for dst, src in LOADS0:
                sp.dma_start(dst, src).then_inc(s_wload0, 16)
            for dst, src in LOADS:
                sp.dma_start(dst, src).then_inc(s_wload, 16)

            def batch(t, b):
                return t[b] if isinstance(b, int) else t[bass.ds(b, 1)].rearrange("a c n -> c (a n)")

            def body(i):
                if here(x_at, i, X_SLOT) and not first_units(i):
                    sp.wait_ge(s_xsplit, 2 * before(x_at, i, 0))
                    sp.dma_start(xs[:, :], batch(x, i + 1)).then_inc(s_xs, 16)
                if here(out0_at, i, OUT_LAG):
                    sp.wait_ge(s_out, before(group_at, i, -PHASE))
                    sp.dma_start(xr[:, :], batch(x, i)).then_inc(s_xr, 16)
                for half, s in ((0, OUT_LAG - PHASE), (1, OUT_LAG - PHASE + GROUP)):
                    cols = slice(half * HALF, (half + 1) * HALF)
                    sp.wait_ge(s_out, before(group_at, i, s + 1 - OUT_LAG + 3))
                    if here(out1_at, i, s):
                        sp.dma_start(batch(y, i - 2)[:, cols], y_sb[:, cols]).then_inc(s_store[half], 16)
                    if here(h_at, i, H_SLOT):
                        sp.dma_start(x1_res[:, cols], x1[:, cols]).then_inc(s_copy[half], 16)

                for s in (s for s, name in UNITS.items() if name[0] == "t" and here(tp_at, i, s)):
                    half = int(UNITS[s][-1])
                    cols = slice(half * HALF, (half + 1) * HALF)
                    sp.wait_ge(s_direct, before(direct_at, i, s) + 1)
                    sp.dma_start(phi2[0:D, :, cols].bitcast(F32), phi2[D:C, :, cols].bitcast(F32)).then_inc(s_phi, 16)

            iterations(sp, body, first=-1)
            for half in range(2):
                sp.wait_ge(s_store[half], 16 * NB)

        @block.tensor
        def _(pe):
            pe.wait_ge(s_weights, 2)

            def product(out, terms, start=True, stop=True):
                for n, (lhs_t, rhs) in enumerate(terms):
                    mm = pe.matmul(out, lhs_t, rhs, start=start and n == 0, stop=stop and n == len(terms) - 1)
                return mm

            def transposes(i, s, half):
                if not here(tile_at, i, s - T_LAG):
                    return
                n = before(tile_at, i, s - T_LAG)
                if half == 0:
                    pe.wait_ge(s_prob, n + 1)
                pe.wait_ge(s_tlo, or_none(2 * n - 1 + half))
                for b in range(GROUP):
                    kb = GROUP * half + b
                    mm = pe.transpose(t_ps[half][:, b * P:(b + 1) * P],
                                      e[:, (s - T_LAG) % 4, kb * P:(kb + 1) * P], ident[:, :])
                mm.then_inc(s_tr, 1)

            def scores(i, s, half):
                if not here(tile_at, i, s):
                    return
                n = before(tile_at, i, s)
                if half == 0:
                    pe.wait_ge(s_exp, or_none(n - 1))
                    if s == 0:
                        pe.wait_ge(s_phi, 16 * before(tp_at, i, 0))
                    if s == PHASE:
                        pe.wait_ge(s_direct, before(direct_at, i, 8))
                    if s == PHASE + GROUP:
                        pe.wait_ge(s_direct, before(direct_at, i, 9))
                out = s_ps[:, s % 2, half * HALF:(half + 1) * HALF]
                t = s % PHASE
                qs, ks = slice(t * P, (t + 1) * P), slice(half * HALF, (half + 1) * HALF)
                if s < PHASE:
                    mm = product(out, [(theta2[:, qs], phi2[:, 0, ks]), (theta2[:, qs], phi2[:, 1, ks])])
                else:
                    mm = product(out, [(q_hi[:, qs], k_hi[:, ks]), (q_hi[:, qs], k_lo[:, ks]),
                                       (q_lo[:, qs], k_hi[:, ks])])
                if half == 1:
                    mm.then_inc(s_scores, 1)

            def values(i, s):
                quarter = (s - PV_LAG) % GROUP
                first = s - PV_LAG - quarter
                if not here(tile_at, i, first):
                    return
                layer = int(first % SLOTS >= PHASE)
                if quarter == 0:
                    pe.wait_ge(s_tlo, 2 * before(tile_at, i, first + GROUP))
                    if s == PV_LAG:
                        pe.wait_ge(s_split, before(values_at, i, 4))
                    if s == PV_LAG + PHASE:
                        pe.wait_ge(s_split, before(values_at, i, 14))
                    pe.wait_ge(s_out, before(group_at, i, first))
                g = first // GROUP % 2
                for kb in (2 * quarter, 2 * quarter + 1):
                    mm = product(o_ps[:, :], [(v_hi[layer][:, kb, :], et_hi[g][:, kb, :]),
                                              (v_lo[layer][:, kb, :], et_hi[g][:, kb, :]),
                                              (v_hi[layer][:, kb, :], et_lo[g][:, kb, :])],
                                 start=kb == 0, stop=kb == KB - 1)
                if quarter == 3:
                    mm.then_inc(s_pv, 1)

            def unit(i, s):
                if not here(unit_at, i, s):
                    return
                name = UNITS[s]
                out = bank(i, s)
                if first_units(i):
                    pe.wait_ge(s_evac, or_none(before(unit_at, i, s) - 1))
                    pe.wait_ge(s_direct, or_none(before(unit_at, i, s) - 1))
                else:
                    pe.wait_ge(s_evac, before(unit_at, i, s))
                    pe.wait_ge(s_direct, before(direct_at, i, s))
                if name == "gn1":
                    pe.wait_ge(s_mv, before(gn1_at, i, s) + 1)
                    mm = pe.matmul(out[:, 0:2], group_avg[:, :], mean_var[:, :], start=True, stop=True)
                elif name == "gn2":
                    pe.wait_ge(s_dev2, before(gn1_at, i, s))
                    mm = pe.matmul(out[:, 0:1], group_avg[:, :], dev2[:, :], start=True, stop=True)
                else:
                    part = int(name[-1])
                    half = part // 2 if name[0] in "vw" else part
                    if name[0] in "tv":
                        pe.wait_ge(s_xsplit, 2 * before(x_at, i, s) - 1 + half)
                        hi, lo, w = x_hi, x_lo, w_hl["tp" if name[0] == "t" else "f"]
                    else:
                        pe.wait_ge(s_h, 2 * before(h_at, i, s) - 1 + half)
                        hi, lo, w = h_hi, h_lo, w_hl[{"k": "k", "q": "q", "w": "pv"}[name[0]]]
                    if name[0] in "vw":
                        for b in range(2):
                            px = slice((2 * part + b) * P, (2 * part + b + 1) * P)
                            pe.matmul(out[:, 2 * b * C:2 * (b + 1) * C], hi[:, px],
                                      w[:, :, :].rearrange("p a c -> p (a c)"), start=True, stop=False)
                            mm = pe.matmul(out[:, 2 * b * C:(2 * b + 1) * C], lo[:, px], w[:, 0, :],
                                           start=False, stop=True)
                    else:
                        px = slice(half * HALF, (half + 1) * HALF)
                        mm = product(out[:, :], [(w[:, 0, :], hi[:, px]), (w[:, 0, :], lo[:, px]),
                                                  (w[:, 1, :], hi[:, px])])
                mm.then_inc(s_unit, 1)

            def body(i):
                for s in range(SLOTS):
                    transposes(i, s, 0)
                    transposes(i, s, 1)
                    scores(i, s, 0)
                    scores(i, s, 1)
                    unit(i, s)
                    values(i, s)

            body(-1)
            pe.wait_ge(s_wload, 16 * len(LOADS))
            pe.wait_ge(s_evac, before(unit_at, 0, 0))
            pe.matmul(o_ps[:, 0:C], v_n[:, :], p_t[:, :], start=True, stop=True)
            pe.matmul(o_ps[:, C:C + 1], p_t[:, :], vec[:, B_V:B_V + 1], start=True, stop=True).then_inc(s_wpv, 1)
            body(0)
            pe.wait_ge(s_weights, len(SPLITS))
            iterations(pe, body, first=1)

        @block.scalar
        def _(act):
            act.wait_ge(s_wload0, 16 * len(LOADS0))
            nc.scalar.activation(w_tp[:, 0:D], w_tp[:, 0:D], ACT.Copy, scale=D ** -0.5).then_inc(s_scaled, 1)
            nc.scalar.activation(vec_ready[0:D, 0:1], vec[0:D, B_TP:B_TP + 1], ACT.Copy,
                                 scale=D ** -0.5).then_inc(s_scaled, 1)
            nc.scalar.activation(vec_ready[D:C, 0:1], vec[D:C, B_TP:B_TP + 1], ACT.Copy).then_inc(s_scaled, 1)
            act.wait_ge(s_scaled, 3)

            def take_hi(i, s, half):
                t = s - T_LAG
                if not here(tile_at, i, t):
                    return
                if half == 0 and t % GROUP == 0:
                    act.wait_ge(s_pv, or_none(before(group_at, i, t) - 1))
                act.wait_ge(s_tr, 2 * before(tile_at, i, t) + 1 + half)
                cols = slice(t % GROUP * P, (t % GROUP + 1) * P)
                nc.scalar.activation(et_hi[t // GROUP % 2][:, GROUP * half:GROUP * (half + 1), cols],
                                     t_ps[half][:, :].rearrange("k (b q) -> k b q", b=GROUP),
                                     ACT.Copy).then_inc(s_thi, 1)

            def take_unit(i, s):
                if not here(unit_at, i, s):
                    return
                name, src = UNITS[s], bank(i, s)
                act.wait_ge(s_unit, before(unit_at, i, s) + 1)
                if name == "gn1":
                    nc.scalar.activation(gmv[:, :], src[:, 0:2], ACT.Copy).then_inc(s_evac, 1)
                    return
                if name == "gn2":
                    nc.scalar.activation(gvar[:, :], src[:, 0:1], ACT.Identity,
                                         bias=gmv[:, 1:2]).then_inc(s_evac, 1)
                    return
                if name[0] == "t":
                    act.wait_ge(s_scores, before(tile_at, i, PHASE))
                    cols = slice(int(name[-1]) * HALF, (int(name[-1]) + 1) * HALF)
                    nc.scalar.activation(theta2[0:D, cols], src[0:D, :], ACT.Identity,
                                         bias=vec_ready[0:D, 0:1]).then_inc(s_theta, 1)
                    nc.scalar.activation(phi2[D:C, 0, cols], src[D:C, :], ACT.Identity,
                                         bias=vec_ready[D:C, 0:1]).then_inc(s_evac, 1)
                elif name[0] in "vw":
                    act.wait_ge(s_split, or_none(before(values_at, i, s) + 1 - STAGES))
                    nc.scalar.activation(stage[:, STAGE[name], :, :, :],
                                         src[:, :].rearrange("p (b t c) -> p b t c", b=2, t=2),
                                         ACT.Copy).then_inc(s_evac, 1)
                else:
                    act.wait_ge(s_scores, before(tile_at, i, 0))
                    cols = slice(int(name[-1]) * HALF, (int(name[-1]) + 1) * HALF)
                    hi, bias = (q_hi, vec_ready[:, 1:2]) if name[0] == "q" else (k_hi, vec[:, B_K:B_K + 1])
                    nc.scalar.activation(hi[:, cols], src[:, :], ACT.Identity, bias=bias).then_inc(s_evac, 1)

            def inputs_hi(i, s):
                if here(h_at, i, s):
                    act.wait_ge(s_gn, before(h_at, i, s) + 1)
                    act.wait_ge(s_unit, before(unit_at, i, 0))
                    nc.scalar.activation(h_hi[:, :], x1[:, :], ACT.Identity, scale=gn_a[:, 0:1],
                                         bias=gn_b[:, 0:1]).then_inc(s_hhi, 1)
                if here(x_at, i, s):
                    act.wait_ge(s_xs, 16 * (before(x_at, i, s) + 1))
                    act.wait_ge(s_unit, before(unit_at, i, 4))
                    nc.scalar.activation(x_hi[:, :], xs[:, :], ACT.Copy).then_inc(s_xhi, 1)

            def exponentials(i, s):
                s = s - 1
                if not here(tile_at, i, s):
                    return
                n = before(tile_at, i, s)
                act.wait_ge(s_max, n + 1)
                act.wait_ge(s_tr, or_none(2 * n - 6))
                nc.scalar.activation(e[:, s % 4, :], s_ps[:, s % 2, :], ACT.Exp, bias=neg_max[:, s % 4:s % 4 + 1],
                                     accum_out=den[:, s % 4:s % 4 + 1]).then_inc(s_exp, 1)

            def body(i):
                for s in range(SLOTS):
                    take_hi(i, s, 0)
                    take_hi(i, s, 1)
                    exponentials(i, s)
                    take_unit(i, s)
                    inputs_hi(i, s)

            body(-1)
            act.wait_ge(s_wload, 16 * len(LOADS))
            nc.scalar.activation(w_q[:, :], w_q[:, :], ACT.Copy, scale=C ** -0.5).then_inc(s_scaled, 1)
            nc.scalar.activation(vec_ready[:, 1:2], vec[:, B_Q:B_Q + 1], ACT.Copy,
                                 scale=C ** -0.5).then_inc(s_scaled, 1)
            act.wait_ge(s_wpv, 1)
            nc.scalar.activation(w_pv[:, :], o_ps[:, 0:C], ACT.Copy).then_inc(s_wpv_sb, 1)
            nc.scalar.activation(vec_ready[:, 2:3], o_ps[:, C:C + 1], ACT.Identity,
                                 bias=vec[:, B_P:B_P + 1]).then_inc(s_scaled, 1)
            act.wait_ge(s_scaled, 6)
            iterations(act, body, first=0)

        @block.vector
        def _(dve):
            def split_weights(n):
                name, w = SPLITS[n]
                nc.vector.tensor_copy(w_hl[name][:, 0, :], w[:, :]).then_inc(s_whi, 1)
                dve.wait_ge(s_whi, n + 1)
                nc.vector.tensor_tensor(w_hl[name][:, 1, :], w[:, :], w_hl[name][:, 0, :].bitcast(F32),
                                        ALU.subtract).then_inc(s_weights, 1)

            dve.wait_ge(s_scaled, 1)
            split_weights(0)
            dve.wait_ge(s_wload0, 16 * len(LOADS0))
            split_weights(1)
            dve.wait_ge(s_scaled, 3)

            def reciprocal(i, s):
                if not here(tile_at, i, s - 2):
                    return
                dve.wait_ge(s_exp, before(tile_at, i, s - 2) + 1)
                c = (s - 2) % 4
                nc.vector.reciprocal(rden[:, c:c + 1], den[:, c:c + 1]).then_inc(s_rden, 1)

            def take_lo(i, s, half):
                t = s - T_LAG
                if not here(tile_at, i, t):
                    return
                dve.wait_ge(s_thi, 2 * before(tile_at, i, t) + 1 + half)
                blocks, cols = slice(GROUP * half, GROUP * (half + 1)), slice(t % GROUP * P, (t % GROUP + 1) * P)
                g = t // GROUP % 2
                nc.vector.tensor_tensor(et_lo[g][:, blocks, cols],
                                        t_ps[half][:, :].rearrange("k (b q) -> k b q", b=GROUP),
                                        et_hi[g][:, blocks, cols].bitcast(F32), ALU.subtract).then_inc(s_tlo, 1)

            def maxima(i, s):
                s = s - 1
                if not here(tile_at, i, s):
                    return
                dve.wait_ge(s_scores, before(tile_at, i, s) + 1)
                nc.vector.tensor_reduce(neg_max[:, s % 4:s % 4 + 1], s_ps[:, s % 2, :], AX.X, ALU.max,
                                        negate=True).then_inc(s_max, 1)

            def outputs(i, s):
                first = s - OUT_LAG
                half = first // GROUP % 2
                cols = slice(half * HALF, (half + 1) * HALF)
                if here(out0_at, i, s):
                    dve.wait_ge(s_pv, before(group_at, i, first) + 1)
                    dve.wait_ge(s_xr, i * 16 + 16)
                    dve.wait_ge(s_h, 2 * before(h_at, i, s))
                    dve.wait_ge(s_hhi, before(h_at, i, s))
                    dve.wait_ge(s_copy[half], 16 * before(h_at, i, s))
                    nc.vector.scalar_tensor_tensor(out=x1[:, cols], in0=o_ps[:, :], scalar=vec[:, B_FUSE:B_FUSE + 1],
                                                   in1=xr[:, cols], op0=ALU.add, op1=ALU.add).then_inc(s_out, 1)
                if here(out1_at, i, s):
                    dve.wait_ge(s_pv, before(group_at, i, first) + 1)
                    n = before(lambda g: out1_at(g) and (g - OUT_LAG) // GROUP % 2 == half, i, s)
                    dve.wait_ge(s_copy[half], 16 * (n + 1))
                    dve.wait_ge(s_store[half], 16 * n)
                    nc.vector.scalar_tensor_tensor(out=y_sb[:, cols], in0=o_ps[:, :], scalar=vec_ready[:, 2:3],
                                                   in1=x1_res[:, cols], op0=ALU.add, op1=ALU.add).then_inc(s_out, 1)

            def statistics(i, s):
                if not here(out0_at, i, s):
                    return
                half = (s - OUT_LAG) // GROUP % 2
                n = before(out0_at, i, s)
                dve.wait_ge(s_out, before(group_at, i, s - OUT_LAG) + 1)
                nc.vector.bn_stats(stats[:, half, :], x1[:, half * HALF:(half + 1) * HALF]).then_inc(s_stats, 1)
                if half == 1:
                    dve.wait_ge(s_stats, n + 1)

            def aggregate(i, s):
                if here(out0_at, i, s) and (s - OUT_LAG) // GROUP % 2 == 1:
                    nc.vector.bn_aggr(mean_var[:, :], stats[:, :, :].rearrange("p a b -> p (a b)")).then_inc(s_mv, 1)

            def unit_lo(i, s):
                s = s - 1
                if not here(direct_at, i, s):
                    return
                name, src = UNITS[s % SLOTS], bank(i, s)
                cols = slice(int(name[-1]) * HALF, (int(name[-1]) + 1) * HALF)
                if name[0] == "t":
                    dve.wait_ge(s_theta, before(tp_at, i, s) + 1)
                    nc.vector.scalar_tensor_tensor(out=theta2[D:C, cols], in0=src[0:D, :],
                                                   scalar=vec_ready[0:D, 0:1], in1=theta2[0:D, cols].bitcast(F32),
                                                   op0=ALU.add, op1=ALU.subtract)
                    hi, lo, bias, rows = phi2[D:C, 0, cols], phi2[D:C, 1, cols], vec_ready[D:C, 0:1], slice(D, C)
                elif name[0] == "q":
                    hi, lo, bias, rows = q_hi[:, cols], q_lo[:, cols], vec_ready[:, 1:2], slice(0, C)
                else:
                    hi, lo, bias, rows = k_hi[:, cols], k_lo[:, cols], vec[:, B_K:B_K + 1], slice(0, C)
                dve.wait_ge(s_evac, before(unit_at, i, s) + 1)
                nc.vector.scalar_tensor_tensor(out=lo, in0=src[rows, :], scalar=bias, in1=hi.bitcast(F32),
                                               op0=ALU.add, op1=ALU.subtract).then_inc(s_direct, 1)

            def body(i):
                for s in range(SLOTS):
                    reciprocal(i, s)
                    maxima(i, s)
                    unit_lo(i, s)
                    outputs(i, s)
                    statistics(i, s)
                    take_lo(i, s, 0)
                    aggregate(i, s)
                    take_lo(i, s, 1)

            body(-1)
            dve.wait_ge(s_scaled, 4)
            split_weights(2)
            dve.wait_ge(s_wload, 16 * len(LOADS))
            split_weights(3)
            dve.wait_ge(s_wpv_sb, 1)
            split_weights(4)
            dve.wait_ge(s_scaled, 6)
            iterations(dve, body, first=0)

        @block.gpsimd
        def _(pool):
            nc.gpsimd.memset(neg_half[:, :], -0.5).then_inc(s_const, 1)
            pool.wait_ge(s_const, 1)
            pool.wait_ge(s_wload0, 16 * len(LOADS0))

            def scaled(*args):
                pool.sem_inc(s_carrier)
                return nc.gpsimd.tensor_scalar(*args)

            def normalise(i, s):
                if not here(tile_at, i, s - 2):
                    return
                pool.wait_ge(s_rden, before(tile_at, i, s - 2) + 1)
                c = (s - 2) % 4
                scaled(e[:, c, :], e[:, c, :], rden[:, c:c + 1], 1.0, ALU.mult,
                                        ALU.mult).then_inc(s_prob, 1)

            def rounded(out, in_, sem):
                scaled(out, in_, 1.0, 1.0, ALU.mult, ALU.mult).then_inc(sem, 1)

            def rest(out, in_, hi, sem):
                nc.gpsimd.tensor_tensor(out, in_, hi.bitcast(F32), ALU.subtract).then_inc(sem, 1)

            def group_norm(i, s):
                if UNITS.get(s) == "gn1" and here(unit_at, i, s):
                    n = before(h_at, i, 0)
                    pool.wait_ge(s_evac, before(unit_at, i, s) + 1)
                    nc.gpsimd.tensor_tensor(dev[:, :], mean_var[:, 0:1], gmv[:, 0:1], ALU.subtract).then_inc(s_dev, 1)
                    pool.wait_ge(s_dev, n + 1)
                    nc.gpsimd.tensor_tensor(dev2[:, :], dev[:, :], dev[:, :], ALU.mult).then_inc(s_dev2, 1)
                if UNITS.get(s) == "gn2" and here(unit_at, i, s):
                    n = before(h_at, i, 0)
                    pool.wait_ge(s_evac, before(unit_at, i, s) + 1)
                    scaled(gvar_eps[:, :], gvar[:, :], EPS, 1.0, ALU.add, ALU.mult).then_inc(s_veps, 1)
                    pool.wait_ge(s_veps, n + 1)
                    nc.gpsimd.tensor_tensor(rstd[:, :], gvar_eps[:, :], neg_half[:, :], ALU.pow).then_inc(s_rstd, 1)
                    pool.wait_ge(s_rstd, n + 1)
                    nc.gpsimd.tensor_tensor(gn_a[:, :], rstd[:, :], vec[:, GN_W:GN_W + 1], ALU.mult).then_inc(s_gna, 1)
                    pool.wait_ge(s_gna, n + 1)
                    nc.gpsimd.tensor_tensor(gn_t[:, :], gmv[:, 0:1], gn_a[:, :], ALU.mult).then_inc(s_gnt, 1)
                    pool.wait_ge(s_gnt, n + 1)
                    nc.gpsimd.tensor_tensor(gn_b[:, :], vec[:, GN_B:GN_B + 1], gn_t[:, :],
                                            ALU.subtract).then_inc(s_gn, 1)

            def inputs_lo(i, s):
                if here(h_at, i, s):
                    n = before(h_at, i, s)
                    pool.wait_ge(s_gn, n + 1)
                    scaled(h[:, :], x1[:, :], gn_a[:, 0:1], gn_b[:, 0:1], ALU.mult,
                                            ALU.add).then_inc(s_h32, 1)
                if s in H_LO_SLOTS and here(h_at, i, H_SLOT):
                    half = H_LO_SLOTS.index(s)
                    cols = slice(half * HALF, (half + 1) * HALF)
                    pool.wait_ge(s_h32, before(h_at, i, s))
                    pool.wait_ge(s_hhi, before(h_at, i, s))
                    rest(h_lo[:, cols], h[:, cols], h_hi[:, cols], s_h)
                if s in X_LO_SLOTS and here(x_at, i, X_SLOT):
                    half = X_LO_SLOTS.index(s)
                    cols = slice(half * HALF, (half + 1) * HALF)
                    pool.wait_ge(s_xhi, before(x_at, i, s))
                    rest(x_lo[:, cols], xs[:, cols], x_hi[:, cols], s_xsplit)

            def split_values(i, s):
                if not here(values_at, i, s - 1):
                    return
                name = UNITS[(s - 1) % SLOTS]
                n = before(values_at, i, s - 1)
                total, part = (stage[:, STAGE[name], :, t, :] for t in range(2))
                pool.wait_ge(s_evac, before(unit_at, i, s - 1) + 1)
                nc.gpsimd.tensor_tensor(total, total, part, ALU.add).then_inc(s_sum, 1)
                pool.wait_ge(s_pv, before(group_at, i, 0) if name[0] == "w"
                             else before(group_at, i, PHASE if s > PHASE else -PHASE))
                values = (v_hi[1], v_lo[1]) if name[0] == "w" else (v_hi[0], v_lo[0])
                hi, lo = (v[:, 2 * int(name[-1]):2 * int(name[-1]) + 2, :] for v in values)
                pool.wait_ge(s_sum, n + 1)
                rounded(hi, total, s_split_hi)
                pool.wait_ge(s_split_hi, n + 1)
                rest(lo, total, hi, s_split)

            def body(i):
                for s in range(SLOTS):
                    normalise(i, s)
                    inputs_lo(i, s)
                    split_values(i, s)
                    group_norm(i, s)

            iterations(pool, body, first=-1)


def kernel(x, L0_conv_W_theta, L0_conv_b_theta, L0_conv_W_phi, L0_conv_b_phi, L0_conv_W_fuse, L0_conv_b_fuse,
           L1_conv_gn_w, L1_conv_gn_b, L1_conv_q_w, L1_conv_q_b, L1_conv_k_w, L1_conv_k_b, L1_conv_v_w,
           L1_conv_v_b, L1_conv_p_w, L1_conv_p_b):
    import numpy as np
    import concourse.bacc as bacc
    from concourse.bass_utils import run_bass_kernel_spmd

    x = np.asarray(x)
    nb, c, hh, ww = x.shape
    per_group = c // GROUPS
    t = lambda w: np.ascontiguousarray(np.asarray(w).T)
    arrays = {
        "x": np.ascontiguousarray(x.reshape(nb, c, hh * ww)),
        "w_theta_t": t(L0_conv_W_theta), "w_phi_t": t(L0_conv_W_phi), "w_fuse_t": t(L0_conv_W_fuse),
        "q_w_t": t(L1_conv_q_w), "k_w_t": t(L1_conv_k_w), "p_w_t": t(L1_conv_p_w),
        "v_w": np.ascontiguousarray(L1_conv_v_w),
        "vectors": np.ascontiguousarray(np.stack(
            [np.concatenate([np.asarray(L0_conv_b_theta), np.asarray(L0_conv_b_phi)])]
            + [np.asarray(v) for v in (L0_conv_b_fuse, L1_conv_q_b, L1_conv_k_b, L1_conv_v_b, L1_conv_p_b,
                                       L1_conv_gn_w, L1_conv_gn_b)], axis=1)),
        "ident": np.eye(c, dtype=np.float32),
        "group_avg": np.kron(np.eye(GROUPS), np.full((per_group, per_group), 1 / per_group)).astype(np.float32),
    }
    nc = bacc.Bacc("TRN2", target_bir_lowering=False, num_devices=1)
    args = [nc.dram_tensor(f"in_{n}", arrays[n].shape, F32, kind="ExternalInput").ap() for n in INS]
    out = nc.dram_tensor("out_y", (nb, c, hh * ww), F32, kind="ExternalOutput").ap()
    attention_pair(nc, *args, out)
    r = run_bass_kernel_spmd(nc, [{f"in_{n}": arrays[n] for n in INS}], core_ids=[0])
    return np.asarray(r.results[0]["out_y"]).reshape(nb, c, hh, ww)
```
